# Optimizing a Trainium2 kernel written in Bass

```python
import numpy as np
import jax
import jax.numpy as jnp

def _softmax(x, axis=-1):
    return jax.nn.softmax(x, axis=axis)

def _gelu(x):
    return jax.nn.gelu(x, approximate=True)

def _silu(x):
    return jax.nn.silu(x)

def _sigmoid(x):
    return jax.nn.sigmoid(x)

def _layernorm(x, axis=-1, eps=1e-05):
    m = jnp.mean(x, axis=axis, keepdims=True)
    v = jnp.var(x, axis=axis, keepdims=True)
    return (x - m) / jnp.sqrt(v + eps)

def _scatter_add(tgt, idx, src, axis=0):
    return tgt.at[idx].add(src)

def _segment_sum(src, seg, n):
    return jax.ops.segment_sum(src, seg, n)
kernel_name = 'mk_gnn_preln_d2_gnn_r8_c543f5'

def setup_inputs(seed: int=0):
    np.random.seed(seed)
    _w = jnp.asarray

    def _rec_inputs():
        import jax
        import jax.numpy as jnp
        _gk = jax.random.key(seed)
        x = -0.0003713 + 1 * jax.random.normal(jax.random.fold_in(_gk, 1), (12500, 128), jnp.float32)
        src = jax.random.randint(jax.random.fold_in(_gk, 2), (400000,), 0, 12500, jnp.int32)
        dst = jnp.minimum((12500 * jax.random.uniform(jax.random.fold_in(_gk, 3), (400000,)) ** 2.0).astype(jnp.int32), 99999)
        _o = jnp.argsort(dst, stable=True)
        src = src[_o]
        dst = dst[_o]
        edge_weight = jax.random.uniform(jax.random.fold_in(_gk, 13), (400000,), jnp.float32, 0.0, 0.999998)
        return (x, src, dst, edge_weight)
    x, src, dst, edge_weight = _rec_inputs()

    def _L0_gnn_setup():
        import jax, jax.numpy as jnp
        import numpy as np
        N_NODES = 12500
        N_EDGES = 125000
        EMB_DIM = 128
        NEG_SLOPE = 0.01
        key = jax.random.key(seed)
        k1, k2, k3, k4 = jax.random.split(key, 4)
        x = jax.random.normal(k1, (N_NODES, EMB_DIM), dtype=jnp.float32)
        edge_index = jax.random.randint(k2, (2, N_EDGES), 0, N_NODES, dtype=jnp.int64)
        edge_attrs = jax.random.uniform(k3, (N_EDGES,), dtype=jnp.float32)
        limit = float(np.sqrt(6.0 / (EMB_DIM + EMB_DIM)))
        W1_w = jax.random.uniform(k4, (EMB_DIM, EMB_DIM), dtype=jnp.float32, minval=-limit, maxval=limit)
        W1_b = jnp.zeros((EMB_DIM,), dtype=jnp.float32)
        return {'x': x, 'edge_index': edge_index, 'edge_attrs': edge_attrs, 'W1_w': W1_w, 'W1_b': W1_b}
    _L0_gnn_all = _L0_gnn_setup()
    _L0_gnn_in = {k: v for k, v in _L0_gnn_all.items() if k in ('W1_w', 'W1_b')}
    del _L0_gnn_all

    def _L1_gnn_setup():
        import jax, jax.numpy as jnp
        import numpy as np
        N_NODES = 12500
        N_EDGES = 200000
        D = 128

        def _sage_conv(h, src, dst, W_self, W_neigh, b):
            n = h.shape[0]
            agg = jax.ops.segment_sum(h[src], dst, num_segments=n)
            deg = jax.ops.segment_sum(jnp.ones_like(dst, dtype=h.dtype), dst, num_segments=n)
            mean_neigh = agg / jnp.maximum(deg, 1.0)[:, None]
            return h @ W_self.T + mean_neigh @ W_neigh.T + b
        key = jax.random.key(seed)
        ks = jax.random.split(key, 9)
        scale = 1.0 / np.sqrt(D)
        return {'x': jax.random.normal(ks[0], (N_NODES, D), dtype=jnp.float32), 'src': jax.random.randint(ks[1], (N_EDGES,), 0, N_NODES, dtype=jnp.int32), 'dst': jax.random.randint(ks[2], (N_EDGES,), 0, N_NODES, dtype=jnp.int32), 'W_self0': jax.random.normal(ks[3], (D, D), dtype=jnp.float32) * scale, 'W_neigh0': jax.random.normal(ks[4], (D, D), dtype=jnp.float32) * scale, 'b0': jnp.zeros((D,), dtype=jnp.float32), 'W_self1': jax.random.normal(ks[5], (D, D), dtype=jnp.float32) * scale, 'W_neigh1': jax.random.normal(ks[6], (D, D), dtype=jnp.float32) * scale, 'b1': jnp.zeros((D,), dtype=jnp.float32)}
    _L1_gnn_all = _L1_gnn_setup()
    _L1_gnn_in = {k: v for k, v in _L1_gnn_all.items() if k in ('W_self0', 'W_neigh0', 'b0', 'W_self1', 'W_neigh1', 'b1')}
    del _L1_gnn_all
    return {'x': x, 'src': src, 'dst': dst, 'edge_weight': edge_weight, 'L0_gnn_W1_w': _L0_gnn_in['W1_w'], 'L0_gnn_W1_b': _L0_gnn_in['W1_b'], 'L1_gnn_W_self0': _L1_gnn_in['W_self0'], 'L1_gnn_W_neigh0': _L1_gnn_in['W_neigh0'], 'L1_gnn_b0': _L1_gnn_in['b0'], 'L1_gnn_W_self1': _L1_gnn_in['W_self1'], 'L1_gnn_W_neigh1': _L1_gnn_in['W_neigh1'], 'L1_gnn_b1': _L1_gnn_in['b1']}

def reference(x, src, dst, edge_weight, L0_gnn_W1_w, L0_gnn_W1_b, L1_gnn_W_self0, L1_gnn_W_neigh0, L1_gnn_b0, L1_gnn_W_self1, L1_gnn_W_neigh1, L1_gnn_b1):
    import jax
    import jax.numpy as jnp

    def _L0_gnn_ref(x, edge_index, edge_attrs, W1_w, W1_b):
        import jax, jax.numpy as jnp
        import numpy as np
        N_NODES = 12500
        N_EDGES = 125000
        EMB_DIM = 128
        NEG_SLOPE = 0.01
        n = x.shape[0]
        from_, to_ = (edge_index[0], edge_index[1])
        deg = jax.ops.segment_sum(jnp.ones((to_.shape[0],), dtype=x.dtype), to_, num_segments=n)
        deg_inv = jnp.where(deg > 0, 1.0 / jnp.sqrt(deg), 0.0)
        norm = deg_inv[from_] * deg_inv[to_]
        x_i = x[from_]
        x_j = x[to_]
        m_j = norm[:, None] * (x_j + x_j * x_i @ W1_w.T + W1_b)
        out = jax.ops.segment_sum(m_j, to_, num_segments=n)
        out = jnp.where(out >= 0, out, NEG_SLOPE * out)
        return out

    def _L1_gnn_ref(x, src, dst, W_self0, W_neigh0, b0, W_self1, W_neigh1, b1):
        import jax, jax.numpy as jnp
        import numpy as np
        N_NODES = 12500
        N_EDGES = 200000
        D = 128

        def _sage_conv(h, src, dst, W_self, W_neigh, b):
            n = h.shape[0]
            agg = jax.ops.segment_sum(h[src], dst, num_segments=n)
            deg = jax.ops.segment_sum(jnp.ones_like(dst, dtype=h.dtype), dst, num_segments=n)
            mean_neigh = agg / jnp.maximum(deg, 1.0)[:, None]
            return h @ W_self.T + mean_neigh @ W_neigh.T + b
        h = _sage_conv(x, src, dst, W_self0, W_neigh0, b0)
        h = jax.nn.relu(h)
        h = _sage_conv(h, src, dst, W_self1, W_neigh1, b1)
        return h
    edge_index = jnp.stack([src, dst])
    h = jnp.maximum(_layernorm(x, axis=-1), 0.0)
    x = x + _L0_gnn_ref(h, edge_index, edge_weight, L0_gnn_W1_w, L0_gnn_W1_b)
    h = jnp.maximum(_layernorm(x, axis=-1), 0.0)
    x = x + _L1_gnn_ref(h, src, dst, L1_gnn_W_self0, L1_gnn_W_neigh0, L1_gnn_b0, L1_gnn_W_self1, L1_gnn_W_neigh1, L1_gnn_b1)
    return x

_drawn_inputs = setup_inputs


def setup_inputs(seed=0):
    import zlib

    import numpy as np

    out = dict(_drawn_inputs(seed))
    spreads = {'L0_gnn_W1_b': (0.0, 0.1), 'L1_gnn_b0': (0.0, 0.1), 'L1_gnn_b1': (0.0, 0.1)}
    factors = {}
    for name, (base, spread) in spreads.items():
        noise = np.random.default_rng([zlib.crc32(name.encode()), seed]).standard_normal(out[name].shape)
        drawn = base * np.exp(spread * noise) if base else spread * noise
        out[name] = jnp.asarray(drawn.astype(out[name].dtype))
    for name, factor in factors.items():
        out[name] = (out[name] * factor).astype(out[name].dtype)
    return out
```

```python
from contextlib import ExitStack

import numpy as np

import concourse.bass as bass
from concourse import mybir

P = 128
CHUNKS = 5
SUBS = 5
GROUP = P * CHUNKS
STEP = GROUP * SUBS
SLOTS = CHUNKS * SUBS
WIN = 64
WIDE = 250
HALF = 7
ROW0 = 132
EPS = 1e-5
SLOPE = 0.01
BANK = 512

ALU = mybir.AluOpType
ACT = mybir.ActivationFunctionType
AX = mybir.AxisListType
F32 = mybir.dt.float32
BF16 = mybir.dt.bfloat16
I32 = mybir.dt.int32
I16 = mybir.dt.int16


def program(nc, x, src, dst, W1, b1, Ws0, Wn0, c0, Ws1, Wn1, c1, out, n_nodes):
    rows = x.shape[0]
    tiles = rows // P
    halves = tiles // HALF
    loops = halves // 2
    iters = src.shape[0] // STEP
    windows = -(-n_nodes // WIDE)
    columns = max(rows, windows * WIDE + WIN, 3 * STEP)
    subs = iters * SUBS
    steps = subs * windows
    DEG, AGG0, AGG1, AGG2 = range(4)
    assert rows == tiles * P and tiles == loops * 2 * HALF and src.shape[0] == iters * STEP and iters <= P

    table0 = nc.dram_tensor("table0", [rows, ROW0], F32).ap()
    table1 = nc.dram_tensor("table1", [rows, P], F32).ap()
    table2 = nc.dram_tensor("table2", [rows, P], F32).ap()
    tables = {AGG0: table0, AGG1: table1, AGG2: table2}

    with ExitStack() as ctx:
        def sb(name, shape, dt=F32):
            return ctx.enter_context(nc.sbuf_tensor(name, shape, dt))

        def sem(name):
            return ctx.enter_context(nc.semaphore(name))

        acc = sb("acc", [P, columns])
        X = sb("X", [P, tiles, P])
        ring = sb("ring", [P, SLOTS, ROW0])
        src_e = sb("src_e", [P, iters, SLOTS], I16)
        dst_e = sb("dst_e", [P, iters, SLOTS], I16)
        idx = sb("idx", [P, SLOTS], I32)
        S = sb("S", [P, SUBS, CHUNKS, WIN])
        Sw = sb("Sw", [P, CHUNKS, WIDE])
        iota_w = sb("iota_w", [P, WIDE])
        cursor = sb("cursor", [P, WIDE])
        row_t = sb("row_t", [tiles, P])
        bases = sb("bases", [1, subs], I32)
        spread = sb("spread", [P, 2])
        spread_all = sb("spread_all", [P, 2])
        fits = sb("fits", [P, 2])
        narrow = sb("narrow", [P, 1])
        narrow_i = sb("narrow_i", [P, 1], I32)
        lowest = sb("lowest", [P, 1])
        base_x = sb("base_x", [P, SUBS, 1])
        ident = sb("ident", [P, P])
        ones_r = sb("ones_r", [1, P])
        ones_b = sb("ones_b", [P, 1], BF16)
        w_t = sb("w_t", [P, 5, P])
        bias_r = sb("bias_r", [1, 3, P])
        bias0 = sb("bias0", [P, P])
        stats = sb("stats", [P, HALF, 6])
        mv_half = sb("mv_half", [P, HALF, 2])
        mv = sb("mv", [P, tiles, 2])
        deg = sb("deg", [P, tiles])
        deg1 = sb("deg1", [P, tiles])
        root = sb("root", [P, tiles])
        dinv = sb("dinv", [P, tiles])
        rdeg = sb("rdeg", [P, tiles])
        rstd = sb("rstd", [P, tiles])
        scale = sb("scale", [P, tiles])
        shift = sb("shift", [P, tiles])
        s0 = sb("s0", [P, tiles])
        s0b = sb("s0b", [P, tiles])
        shared = sb("shared", [P, columns])
        place = [0]

        def part(*shape):
            n = int(np.prod(shape))
            a = shared[:, place[0]:place[0] + n]
            place[0] += n
            names = "abc"[:len(shape)]
            return a.rearrange(f"p ({' '.join(names)}) -> p {' '.join(names)}", **dict(zip(names, shape)))

        tin = part(2, HALF, ROW0)
        tout = part(2, HALF, ROW0)
        hT = part(HALF, P)
        aT = part(HALF, P)
        u = part(HALF, P)
        v = part(HALF, P)
        w_in = part(5, P)
        row_of = {0: acc[0:1, :], 1: shared[0:1, :]}
        ps = ctx.enter_context(nc.psum_tensor("ps", [P, 8, BANK], F32))


        dst_i, dst_n, src_i = (acc[0:iters, k * STEP:(k + 1) * STEP] for k in range(3))
        dst_i, src_i = dst_i.bitcast(I32), src_i.bitcast(I32)
        src_n = ring[0:iters, :, :].rearrange("i k f -> i (k f)")[:, 0:STEP]
        Sb, Swb = (a.bitcast(BF16) for a in (S[:, :, :, :], Sw[:, :, :]))
        Sb, Swb = Sb[:, :, :, 0:WIN], Swb[:, :, 0:WIDE]

        s_edges = sem("s_edges")
        s_x = sem("s_x")
        s_w = sem("s_w")
        s_const = sem("s_const")
        s_iden = sem("s_iden")
        s_prep = sem("s_prep")
        s_all = sem("s_all")
        s_nat = sem("s_nat")
        s_turn = sem("s_turn")
        s_turned = sem("s_turned")
        s_narrow = sem("s_narrow")
        s_zero = sem("s_zero")
        s_S = sem("s_S")
        s_done = sem("s_done")
        s_flush = sem("s_flush")
        s_idx = sem("s_idx")
        s_gather = [sem(f"s_gather{k}") for k in range(SLOTS)]
        s_Sw = [sem(f"s_Sw{k}") for k in range(4)]
        s_sum = [sem(f"s_sum{k}") for k in range(4)]
        s_own = [sem(f"s_own{k}") for k in range(4)]
        s_row = sem("s_row")
        s_rowt = sem("s_rowt")
        s_small = sem("s_small")
        s_sqrt_in = sem("s_sqrt_in")
        s_sqrt = sem("s_sqrt")
        s_norm = sem("s_norm")
        s_stat = sem("s_stat")
        s_store = [sem(f"s_store{h}") for h in range(2)]
        s_tout = sem("s_tout")
        s_load = [sem(f"s_load{h}") for h in range(2)]
        s_tin = sem("s_tin")
        s_hps = sem("s_hps")
        s_hT = sem("s_hT")
        s_aT = sem("s_aT")
        s_mm = sem("s_mm")
        s_psfree = sem("s_psfree")
        s_v = [sem(f"s_v{k}") for k in range(3)]
        s_pre = sem("s_pre")
        s_apart = {e: sem(f"s_apart_{e.name}") for e in (mybir.EngineType.Pool, mybir.EngineType.PE, mybir.EngineType.DVE)}

        def apart(eng):
            eng.sem_inc(s_apart[eng.engine])

        FLUSHED = SUBS

        def tile_rows(t, table, width, count=HALF):
            return table[bass.ds(t * P, count * P), 0:width].rearrange("(t p) f -> p t f", p=P)

        block = ctx.enter_context(nc.Block())

        @block.sync
        def _(sp):
            sp.dma_start(dst_i, dst.rearrange("(i e) -> i e", e=STEP)).then_inc(s_edges, 16)
            sp.dma_start(src_i, src.rearrange("(i e) -> i e", e=STEP)).then_inc(s_edges, 16)
            with nc.allow_non_contiguous_dma(reason="one word of each subgroup"):
                sp.dma_start(bases[:, :], dst.rearrange("(a s e) -> a s e", a=1, e=GROUP)[:, :, 0]).then_inc(s_edges, 16)
            for i in range(loops):
                t = 2 * HALF * i
                sp.dma_start(X[:, t:t + 2 * HALF, :],
                             x[t * P:(t + 2 * HALF) * P, :].rearrange("(t p) f -> p t f", p=P)).then_inc(s_x, 16)
            for k, w in enumerate((W1, Ws0, Wn0, Ws1, Wn1)):
                sp.dma_start(w_in[:, k, :], w).then_inc(s_w, 16)
            for k, b in enumerate((b1, c0, c1)):
                sp.dma_start(bias_r[:, k, :], b.rearrange("(a f) -> a f", a=1)).then_inc(s_w, 16)

            def spread_row(nth):
                sp.wait_ge(s_row, nth)
                sp.dma_start(row_t[:, :], row_of[nth - 1][:, 0:rows].rearrange("a (t p) -> a t p", p=P)).then_inc(s_rowt, 16)
                sp.wait_ge(s_rowt, 16 * nth)

            def store(nth, table, width):
                with sp.Fori(0, loops) as i:
                    for h in range(2):
                        sp.wait_ge(s_tout, (nth * loops + i) * 2 + h + 1)
                        d = sp.dma_start(tile_rows(i * 2 * HALF + h * HALF, table, width), tout[:, h, :, 0:width])
                        d.then_inc(s_store[h], 16)

            def load(nth, of, width):
                with sp.Fori(0, loops) as i:
                    for h in range(2):
                        sp.wait_ge(s_tin, (nth * loops + i) * 2 + h + 1)
                        sp.dma_start(tin[:, h, :, 0:width], tile_rows(i * 2 * HALF + h * HALF, of, width)).then_inc(s_load[h], 16)

            spread_row(1)
            store(0, table0, ROW0)
            for h in range(2):
                sp.wait_ge(s_store[h], 16 * loops)
            spread_row(2)
            load(0, table0, ROW0)
            store(1, table1, P)
            for h in range(2):
                sp.wait_ge(s_store[h], 32 * loops)
            load(1, table1, P)
            for h in range(2):
                sp.wait_ge(s_store[h], 48 * loops)
            load(2, table2, P)

        @block.scalar
        def _(act):
            def root_of(nth):
                act.wait_ge(s_sqrt_in, nth)
                act.activation(root[:, :], root[:, :], ACT.Sqrt).then_inc(s_sqrt, 1)

            def normalise(nth):
                act.wait_ge(s_norm, nth + 1)

                def both(i, first):
                    for h in range(2):
                        if not first:
                            act.wait_ge(s_store[h], (nth * loops + i) * 16)
                        for j in range(HALF):
                            t = i * 2 * HALF + h * HALF + j
                            a = act.activation(tout[:, h, j, 0:P], X[:, bass.ds(t, 1), :].rearrange("p a f -> p (a f)"), ACT.Relu,
                                               bias=shift[:, bass.ds(t, 1)], scale=scale[:, bass.ds(t, 1)])
                        if nth == 0:
                            a = act.activation(tout[:, h, :, P:P + 1],
                                               dinv[:, bass.ds(i * 2 * HALF + h * HALF, HALF)].unsqueeze(2), ACT.Copy)
                        a.then_inc(s_tout, 1)

                if nth == 0:
                    both(0, True)
                with act.Fori(1 if nth == 0 else 0, loops) as i:
                    both(i, False)

            def indices(nth):
                with act.Fori(0, iters) as i:
                    for s in range(SUBS):
                        act.wait_ge(s_done, nth * subs + i * SUBS + s + 1)
                        act.activation(idx[:, s * CHUNKS:(s + 1) * CHUNKS],
                                       src_e[:, bass.ds(i, 1), s * CHUNKS:(s + 1) * CHUNKS].rearrange("p a c -> p (a c)"),
                                       ACT.Copy).then_inc(s_idx, 1)

            def sage(nth, to):
                act.wait_ge(s_flush, FLUSHED + (nth + 2) * subs)
                with act.Fori(0, loops) as i:
                    for h in range(2):
                        n = (nth - 1) * 2 * loops + i * 2 + h
                        act.wait_ge(s_mm, (nth * loops + i) * 2 + h + 1)
                        act.activation(aT[:, :, :].rearrange("p t f -> p (t f)"),
                                       acc[:, bass.ds((i * 2 + h) * HALF * P, HALF * P)], ACT.Copy).then_inc(s_aT, 1)
                        act.wait_ge(s_pre, n + 1)
                        act.wait_ge(s_store[h], ((nth + 1) * loops + i) * 16)
                        act.activation(tout[:, h, :, 0:P], u[:, :, :], ACT.Relu if nth == 1 else ACT.Copy).then_inc(s_tout, 1)
                        act.wait_ge(s_tout, ((nth + 1) * loops + i) * 2 + h + 1)
                        act.dma_start(tile_rows((i * 2 + h) * HALF, to, P), tout[:, h, :, 0:P]).then_inc(s_store[h], 16)

            root_of(1)
            root_of(2)
            act.wait_ge(s_const, 1)
            normalise(0)
            act.wait_ge(s_turned, 2 * 7)
            indices(AGG0)
            root_of(3)
            normalise(1)
            indices(AGG1)
            sage(1, table2)
            indices(AGG2)
            sage(2, out)
            for h in range(2):
                act.wait_ge(s_store[h], 4 * loops * 16)

        @block.gpsimd
        def _(pool):
            pool.memset(ident[:, :], 0.0).then_inc(s_iden, 1)
            pool.memset(spread[:, :], 0.0).then_inc(s_iden, 1)
            pool.memset(ones_r[:, :], 1.0)
            pool.memset(ones_b[:, :], 1.0)
            pool.iota(iota_w[:, :], pattern=[[1, WIDE]], base=0, channel_multiplier=0, allow_small_or_imprecise_dtypes=True)
            pool.memset(tout[:, :, :, :], 0.0)
            pool.wait_ge(s_iden, 1)
            pool.affine_select(out=ident[:, :], in_=ident[:, :], compare_op=ALU.not_equal, fill=1.0,
                               base=0, pattern=[[-1, P]], channel_multiplier=1).then_inc(s_const, 1)
            pool.wait_ge(s_prep, 5)
            pool.partition_all_reduce(spread_all[:, :], spread[:, :], P, bass.bass_isa.ReduceOp.max).then_inc(s_all, 1)

            for nth in (AGG0, AGG1, AGG2):
                table = tables[nth]
                width = ROW0 if nth == AGG0 else P
                for h in range(2):
                    pool.wait_ge(s_store[h], nth * loops * 16)
                with pool.Fori(0, iters) as i:
                    for s in range(SUBS):
                        pool.wait_ge(s_idx, ((nth - 1) * iters + i) * SUBS + s + 1)
                        apart(pool)
                        for k in range(s * CHUNKS, (s + 1) * CHUNKS):
                            pool.indirect_dma_start(ring[:, k, 0:width], None, table,
                                                    bass.IndirectOffsetOnAxis(ap=idx[:, k:k + 1], axis=0)).then_inc(s_gather[k], 16)

        @block.tensor
        def _(pe):
            def bank(k, a, b, p=P):
                return ps[0:p, k, a:b]

            pe.wait_ge(s_const, 1)
            done = 0
            for which, of in enumerate((src_n, dst_n)):
                pe.wait_ge(s_nat, which + 1)
                for first in range(0, SLOTS, 4):
                    if done >= 7:
                        pe.wait_ge(s_turned, done - 6)
                    for j, sc in enumerate(range(first, min(first + 4, SLOTS))):
                        s, c = divmod(sc, CHUNKS)
                        part = of[:, s * GROUP:(s + 1) * GROUP].rearrange("i (p c) -> i p c", c=CHUNKS)[:, :, c]
                        t = pe.transpose(bank(done % 7, j * iters, (j + 1) * iters), part, ident[0:iters, 0:iters])
                    t.then_inc(s_turn, 1)
                    done += 1
            pe.wait_ge(s_w, 8 * 16)
            pe.wait_ge(s_turned, done)
            for k in range(5):
                t = pe.transpose(bank(k // 4, (k % 4) * P, (k % 4 + 1) * P), w_in[:, k, :], ident[:, :])
            pe.matmul(bank(2, 0, P), ones_r[:, :], bias_r[:, 0, :], start=True, stop=True).then_inc(s_turn, 1)
            pe.wait_ge(s_narrow, 1)
            is_narrow = pe.value_load(narrow_i[0:1, 0:1], min_val=0, max_val=1)
            pe.wait_ge(s_turned, done + 1)
            pe.sem_inc(s_done, SUBS)
            pe.sem_inc(s_mm, 1)

            def products(nth, s, onehots, out_f, out_r):
                for c in range(CHUNKS):
                    k, st = s * CHUNKS + c, dict(start=c == 0, stop=c == CHUNKS - 1)
                    if nth == DEG:
                        m = pe.matmul(out_r, ones_b[:, :], onehots[:, c, :], **st)
                    else:
                        m = pe.matmul(out_f, ring[:, k, 0:P], onehots[:, c, :], **st)
                if nth == AGG0:
                    for c in range(CHUNKS):
                        k, st = s * CHUNKS + c, dict(start=c == 0, stop=c == CHUNKS - 1)
                        m = pe.matmul(out_r, ring[:, k, P:P + 1], onehots[:, c, :], **st)
                return m

            def edges(nth):
                one, wide = (Sb, Swb) if nth == DEG else (S, Sw)

                def gathered(i, s):
                    if nth != DEG:
                        for k in range(s * CHUNKS, (s + 1) * CHUNKS):
                            pe.wait_ge(s_gather[k], ((nth - 1) * iters + i + 1) * 16)

                with pe.If(is_narrow):
                    with pe.Fori(0, iters) as i:
                        for s in range(SUBS):
                            n = nth * subs + i * SUBS + s + 1
                            pe.wait_ge(s_S, n)
                            pe.wait_ge(s_flush, n)
                            gathered(i, s)
                            products(nth, s, one[:, s, :, :], bank(s, 0, WIN), bank(s, WIN, 2 * WIN, 1)).then_inc(s_done, 1)
                with pe.Else():
                    with pe.Fori(0, iters) as i:
                        for s in range(SUBS):
                            gathered(i, s)
                            apart(pe)
                            with pe.Fori(0, windows) as w:
                                n = (i * SUBS + s) * windows + w
                                pe.wait_ge(s_Sw[nth], n + 1)
                                products(nth, s, wide[:, :, :], bank(5, 0, WIDE), bank(6, 0, WIDE, 1)).then_inc(s_sum[nth], 1)
                            pe.wait_ge(s_sum[nth], (i * SUBS + s + 1) * windows)
                            pe.sem_inc(s_done, 1)

            def turn_row(nth):
                pe.wait_ge(s_rowt, 16 * nth)
                pe.transpose(bank(7, 0, tiles), row_t[:, :], ident[0:tiles, 0:tiles]).then_inc(s_turn, 1)

            def layer(nth):
                pe.wait_ge(s_flush, FLUSHED + (nth + 2) * subs)
                with pe.Fori(0, loops) as i:
                    for h in range(2):
                        n = (nth * loops + i) * 2 + h
                        pe.wait_ge(s_load[h], (nth * loops + i + 1) * 16)
                        pe.wait_ge(s_psfree, n + 1)
                        for j in range(HALF):
                            t = pe.transpose(bank(j, 0, P), tin[:, h, j, 0:P], ident[:, :])
                        t.then_inc(s_hps, 1)
                        pe.wait_ge(s_hT, n + 1)
                        if nth:
                            pe.wait_ge(s_aT, n - 2 * loops + 1)
                        for j in range(HALF):
                            if nth == 0:
                                m = pe.matmul(bank(j, P, 2 * P), hT[:, j, :], w_t[:, 0, :], start=True, stop=True)
                            else:
                                pe.matmul(bank(j, P, 2 * P), hT[:, j, :], w_t[:, 2 * nth - 1, :], start=True, stop=False)
                                pe.matmul(bank(j, P, 2 * P), ones_r[:, :], bias_r[:, nth, :], start=False, stop=True)
                                m = pe.matmul(bank(j, 2 * P, 3 * P), aT[:, j, :], w_t[:, 2 * nth, :], start=True, stop=True)
                        m.then_inc(s_mm, 1)

            edges(DEG)
            turn_row(1)
            edges(AGG0)
            turn_row(2)
            layer(0)
            edges(AGG1)
            layer(1)
            edges(AGG2)
            layer(2)

        @block.vector
        def _(dve):
            dve.wait_ge(s_edges, 48)
            dve.wait_ge(s_iden, 2)
            dve.tensor_copy(dst_n, dst_i).then_inc(s_prep, 1)
            dve.tensor_copy(src_n, src_i).then_inc(s_nat, 1)
            dve.wait_ge(s_prep, 1)
            by_sub = dst_n.rearrange("i (s e) -> i s e", e=GROUP)
            rel = dst_i.bitcast(F32).rearrange("i (s e) -> i s e", e=GROUP)
            dve.tensor_tensor(rel, by_sub, by_sub[:, :, 0:1].to_broadcast([iters, SUBS, GROUP]), ALU.subtract).then_inc(s_prep, 1)
            dve.wait_ge(s_prep, 2)
            dve.tensor_reduce(spread[0:iters, 0:1], rel, AX.XY, ALU.max).then_inc(s_prep, 1)
            dve.tensor_reduce(lowest[0:iters, :], rel, AX.XY, ALU.min).then_inc(s_prep, 1)
            dve.wait_ge(s_prep, 4)
            dve.tensor_scalar(spread[0:iters, 1:2], lowest[0:iters, :], -1.0, None, ALU.mult).then_inc(s_prep, 1)
            dve.wait_ge(s_all, 1)
            dve.tensor_scalar(fits[:, 0:1], spread_all[:, 0:1], float(WIN - 1), None, ALU.is_le).then_inc(s_prep, 1)
            dve.tensor_scalar(fits[:, 1:2], spread_all[:, 1:2], 0.0, None, ALU.is_le).then_inc(s_prep, 1)
            dve.wait_ge(s_prep, 7)
            dve.tensor_tensor(narrow[:, :], fits[:, 0:1], fits[:, 1:2], ALU.mult).then_inc(s_prep, 1)
            dve.wait_ge(s_prep, 8)
            dve.tensor_copy(narrow_i[:, :], narrow[:, :]).then_inc(s_narrow, 1)
            dve.tensor_scalar(base_x[0:iters], by_sub[:, :, 0:1], narrow[0:iters, 0:1], None, ALU.mult).then_inc(s_prep, 1)
            dve.wait_ge(s_prep, 9)
            dve.tensor_tensor(by_sub, by_sub, base_x[0:iters].to_broadcast([iters, SUBS, GROUP]), ALU.subtract).then_inc(s_nat, 1)
            done = 0
            for to in (src_e, dst_e):
                for first in range(0, SLOTS, 4):
                    k = min(4, SLOTS - first)
                    dve.wait_ge(s_turn, done + 1)
                    dve.tensor_copy(to[:, :, first:first + k].rearrange("p i k -> p k i"),
                                    ps[:, done % 7, 0:k * iters].rearrange("p (k i) -> p k i", k=k)).then_inc(s_turned, 1)
                    done += 1
            dve.wait_ge(s_turn, done + 1)
            dve.tensor_copy(w_t[:, 0:4, :], ps[:, 0, :].rearrange("p (k f) -> p k f", f=P))
            dve.tensor_copy(w_t[:, 4, :], ps[:, 1, 0:P])
            dve.tensor_copy(bias0[:, :], ps[:, 2, 0:P]).then_inc(s_turned, 1)
            turned = done + 1

            small = [0]

            def own(ins):
                small[0] += 1
                ins.then_inc(s_small, 1)
                dve.wait_ge(s_small, small[0])

            def square_root(nth, arg):
                arg.then_inc(s_sqrt_in, 1)
                dve.wait_ge(s_sqrt, nth)

            is_narrow = dve.value_load(narrow_i[0:1, 0:1], min_val=0, max_val=1)
            dve.sem_inc(s_flush, SUBS)
            dve.sem_inc(s_psfree, 1)
            dve.sem_inc(s_tin, 2)

            def edges(nth):
                one, wide = (Sb, Swb) if nth == DEG else (S, Sw)
                row = row_of.get(nth)
                if nth == AGG0:
                    for h in range(2):
                        dve.wait_ge(s_store[h], 16 * loops)
                if row is not None:
                    own(dve.memset(row, 0.0))
                if nth != DEG:
                    own(dve.memset(acc[:, :], 0.0))

                def onehots(to, i, s, cols):
                    n = to.shape[2]
                    at = dst_e[:, bass.ds(i, 1), s * CHUNKS:(s + 1) * CHUNKS].rearrange("p a c -> p (a c)")
                    return dve.tensor_tensor(to, at.unsqueeze(2).to_broadcast([P, CHUNKS, n]),
                                             cols.unsqueeze(1).to_broadcast([P, CHUNKS, n]), ALU.is_equal)

                def add(base, width, k_f, k_r, at_r):
                    if nth != DEG:
                        a = dve.tensor_tensor(acc[:, bass.ds(base, width)], acc[:, bass.ds(base, width)], ps[:, k_f, 0:width], ALU.add)
                    if nth in (DEG, AGG0):
                        a = dve.tensor_tensor(row[:, bass.ds(base, width)], row[:, bass.ds(base, width)],
                                              ps[0:1, k_r, at_r:at_r + width], ALU.add)
                    return a

                with dve.If(is_narrow):
                    regs = [dve.alloc_register(f"base{nth}_{s}") for s in range(SUBS)]
                    with dve.Fori(0, iters) as i:
                        dve.load(regs, bases[0:1, bass.ds(i * SUBS, SUBS)])
                        base = [dve.snap(r, min_val=0, max_val=n_nodes - 1) for r in regs]
                        for s in range(SUBS):
                            n = nth * subs + i * SUBS + s + 1
                            dve.wait_ge(s_done, n)
                            onehots(one[:, s, :, :], i, s, iota_w[:, 0:WIN]).then_inc(s_S, 1)
                        for s in range(SUBS):
                            n = nth * subs + i * SUBS + s + 1
                            dve.wait_ge(s_flush, n + SUBS - 1)
                            dve.wait_ge(s_done, n + SUBS)
                            add(base[s], WIN, s, s, WIN).then_inc(s_flush, 1)
                with dve.Else():
                    with dve.Fori(0, iters) as i:
                        for s in range(SUBS):
                            dve.tensor_copy(cursor[:, :], iota_w[:, :]).then_inc(s_own[nth], 1)
                            with dve.Fori(0, windows) as w:
                                n = (i * SUBS + s) * windows + w
                                own_n = (i * SUBS + s) * (windows + 1) + w + 1
                                dve.wait_ge(s_own[nth], own_n)
                                onehots(wide[:, :, :], i, s, cursor[:, :]).then_inc(s_Sw[nth], 1)
                                dve.wait_ge(s_Sw[nth], n + 1)
                                dve.wait_ge(s_sum[nth], n + 1)
                                add(w * WIDE, WIDE, 5, 6, 0)
                                dve.tensor_scalar(cursor[:, :], cursor[:, :], float(WIDE), None, ALU.add).then_inc(s_own[nth], 1)
                            dve.wait_ge(s_own[nth], (i * SUBS + s + 1) * (windows + 1))
                            dve.sem_inc(s_flush, 1)

            def column_of_row(nth, to):
                dve.wait_ge(s_flush, FLUSHED + nth * subs)
                dve.sem_inc(s_row, 1)
                dve.wait_ge(s_turn, turned + nth)
                own(dve.tensor_copy(to, ps[:, 7, 0:tiles]))

            def statistics(t, first):
                for j in range(HALF):
                    dve.bn_stats(stats[:, j, :], X[:, bass.ds(t + j, 1), :].rearrange("p a f -> p (a f)")).then_inc(s_stat, 1)
                dve.wait_ge(s_stat, first + HALF)
                apart(dve)
                for j in range(HALF):
                    a = dve.bn_aggr(mv_half[:, j, :], stats[:, j, :])
                a.then_inc(s_stat, 1)
                dve.wait_ge(s_stat, first + HALF + 1)
                dve.tensor_copy(mv[:, bass.ds(t, HALF), :], mv_half[:, :, :]).then_inc(s_stat, 1)
                dve.wait_ge(s_stat, first + HALF + 2)

            dve.wait_ge(s_x, loops * 16)
            with dve.Fori(0, halves) as i:
                statistics(i * HALF, i * (HALF + 2))

            edges(DEG)
            column_of_row(1, deg[:, :])
            own(dve.tensor_scalar(deg1[:, :], deg[:, :], 1.0, None, ALU.max))
            own(dve.reciprocal(rdeg[:, :], deg1[:, :]))
            square_root(1, dve.tensor_copy(root[:, :], deg1[:, :]))
            own(dve.reciprocal(dinv[:, :], root[:, :]))
            own(dve.tensor_scalar(deg[:, :], deg[:, :], 1.0, None, ALU.min))
            own(dve.tensor_tensor(dinv[:, :], dinv[:, :], deg[:, :], ALU.mult))

            def norm(nth, root_nth, times=None):
                square_root(root_nth, dve.tensor_scalar(root[:, :], mv[:, :, 1], EPS, None, ALU.add))
                own(dve.reciprocal(rstd[:, :], root[:, :]))
                if times is not None:
                    own(dve.tensor_tensor(scale[:, :], rstd[:, :], times, ALU.mult))
                else:
                    own(dve.tensor_copy(scale[:, :], rstd[:, :]))
                dve.scalar_tensor_tensor(shift[:, :], mv[:, :, 0], -1.0, scale[:, :], ALU.mult, ALU.mult).then_inc(s_norm, 1)

            norm(0, 2, dinv[:, :])

            def chain(sem_of, start):
                q = [start]

                def then(ins):
                    q[0] = q[0] + 1
                    ins.then_inc(sem_of, 1)
                    dve.wait_ge(sem_of, q[0])
                return then

            def per_node(a, t):
                return a[:, bass.ds(t, HALF)].unsqueeze(2).to_broadcast([P, HALF, P])

            edges(AGG0)
            column_of_row(2, s0[:, :])
            own(dve.tensor_tensor(s0b[:, :], s0[:, :], dinv[:, :], ALU.mult))
            with dve.Fori(0, loops) as i:
                for h in range(2):
                    n = i * 2 + h
                    t = n * HALF
                    then = chain(s_v[0], n * 6)
                    dve.wait_ge(s_hps, n + 1)
                    dve.wait_ge(s_mm, n + 1)
                    dve.tensor_tensor(hT[:, :, :], ps[:, 0:HALF, 0:P],
                                      acc[:, bass.ds(t * P, HALF * P)].rearrange("p (t n) -> p t n", n=P), ALU.mult).then_inc(s_hT, 1)
                    then(dve.tensor_tensor(v[:, :, :], tin[:, h, :, 0:P], per_node(s0, t), ALU.mult))
                    dve.sem_inc(s_tin, 1)
                    then(dve.tensor_tensor(u[:, :, :], bias0[:, :].unsqueeze(1).to_broadcast([P, HALF, P]), per_node(s0b, t), ALU.mult))
                    then(dve.tensor_tensor(v[:, :, :], v[:, :, :], u[:, :, :], ALU.add))
                    dve.wait_ge(s_mm, n + 2)
                    then(dve.tensor_tensor(v[:, :, :], v[:, :, :], ps[:, 0:HALF, P:2 * P], ALU.add))
                    dve.sem_inc(s_psfree, 1)
                    then(dve.scalar_tensor_tensor(u[:, :, :], v[:, :, :], SLOPE, v[:, :, :], ALU.mult, ALU.max))
                    then(dve.tensor_tensor(X[:, bass.ds(t, HALF), :], X[:, bass.ds(t, HALF), :], u[:, :, :], ALU.add))
                    apart(dve)
                    statistics(t, (halves + n) * (HALF + 2))
            norm(1, 3)

            for nth, agg in ((1, AGG1), (2, AGG2)):
                edges(agg)
                with dve.Fori(0, loops) as i:
                    for h in range(2):
                        n = (nth * loops + i) * 2 + h
                        t = (i * 2 + h) * HALF
                        then = chain(s_v[nth], (i * 2 + h) * nth)
                        dve.wait_ge(s_hps, n + 1)
                        dve.sem_inc(s_tin, 1)
                        dve.wait_ge(s_mm, n + 1)
                        dve.tensor_copy(hT[:, :, :], ps[:, 0:HALF, 0:P]).then_inc(s_hT, 1)
                        dve.wait_ge(s_mm, n + 2)
                        then(dve.tensor_tensor(v[:, :, :], ps[:, 0:HALF, 2 * P:3 * P], per_node(rdeg, t), ALU.mult))
                        dve.wait_ge(s_tout, ((nth + 1) * loops + i) * 2 + h)
                        if nth == 2:
                            then(dve.tensor_tensor(v[:, :, :], v[:, :, :], X[:, bass.ds(t, HALF), :], ALU.add))
                        dve.tensor_tensor(u[:, :, :], v[:, :, :], ps[:, 0:HALF, P:2 * P], ALU.add).then_inc(s_pre, 1)
                        dve.wait_ge(s_pre, (n - 2 * loops) + 1)
                        dve.sem_inc(s_psfree, 1)


_INS = ["x", "src", "dst", "L0_gnn_W1_w", "L0_gnn_W1_b", "L1_gnn_W_self0", "L1_gnn_W_neigh0", "L1_gnn_b0",
        "L1_gnn_W_self1", "L1_gnn_W_neigh1", "L1_gnn_b1"]


def kernel(**inputs):
    import concourse.bacc as bacc
    from concourse.bass_utils import run_bass_kernel_spmd

    nc = bacc.Bacc("TRN2", target_bir_lowering=False, num_devices=1)
    n_nodes = inputs["x"].shape[0]
    block = 2 * HALF * P
    rows = -(-n_nodes // block) * block
    arrays, args = {}, []
    for name in _INS:
        a = np.ascontiguousarray(inputs[name])
        if name == "x":
            a = np.concatenate([a, np.zeros((rows - n_nodes, P), a.dtype)])
        arrays[f"in_{name}"] = a
        args.append(nc.dram_tensor(f"in_{name}", a.shape, mybir.dt.from_np(a.dtype), kind="ExternalInput").ap())
    args.append(nc.dram_tensor("out", (rows, P), F32, kind="ExternalOutput").ap())
    program(nc, *args, n_nodes)
    r = run_bass_kernel_spmd(nc, [arrays], core_ids=[0])
    return r.results[0]["out"][:n_nodes]
```
